# Optimizing a Trainium2 kernel written in Bass

```python
import numpy as np
import jax
import jax.numpy as jnp

def _softmax(x, axis=-1):
    return jax.nn.softmax(x, axis=axis)
def _gelu(x):
    return jax.nn.gelu(x, approximate=True)
def _silu(x):
    return jax.nn.silu(x)
def _sigmoid(x):
    return jax.nn.sigmoid(x)
def _layernorm(x, axis=-1, eps=1e-5):
    m = jnp.mean(x, axis=axis, keepdims=True)
    v = jnp.var(x, axis=axis, keepdims=True)
    return (x - m) / jnp.sqrt(v + eps)
def _scatter_add(tgt, idx, src, axis=0):
    return tgt.at[idx].add(src)
def _segment_sum(src, seg, n):
    return jax.ops.segment_sum(src, seg, n)

kernel_name = 'mk_conv_seq_d2_conv_nchw256_1a2510'

def setup_inputs(seed: int = 0):
    np.random.seed(seed)
    _w = jnp.asarray
    def _rec_inputs():
        import jax
        import jax.numpy as jnp
        _gk = jax.random.key(seed)
        x = -0.0002023 + 1 * jax.random.normal(jax.random.fold_in(_gk, 1), (8, 256, 56, 56), jnp.float32)
        return x
    x = _rec_inputs()
    def _L0_conv_setup():
        import jax, jax.numpy as jnp
        import numpy as np
        BN_EPS = 1e-05

        def conv1x1(x, w, b):
            return jnp.einsum('bchw,oc->bohw', x, w) + b[None, :, None, None]
        key = jax.random.key(seed)
        ks = jax.random.split(key, 10)
        B, C, H, W = (8, 256, 56, 56)
        DI, DO = (128, 256)
        s_in = 1.0 / np.sqrt(C)
        s_inner = 1.0 / np.sqrt(DI)
        return {'x': jax.random.normal(ks[0], (B, C, H, W), jnp.float32), 'theta_w': jax.random.normal(ks[1], (DI, C), jnp.float32) * s_in, 'theta_b': jax.random.normal(ks[2], (DI,), jnp.float32) * 0.01, 'phi_w': jax.random.normal(ks[3], (DI, C), jnp.float32) * s_in, 'phi_b': jax.random.normal(ks[4], (DI,), jnp.float32) * 0.01, 'g_w': jax.random.normal(ks[5], (DI, C), jnp.float32) * s_in, 'g_b': jax.random.normal(ks[6], (DI,), jnp.float32) * 0.01, 'out_w': jax.random.normal(ks[7], (DO, DI), jnp.float32) * s_inner, 'out_b': jax.random.normal(ks[8], (DO,), jnp.float32) * 0.01, 'bn_gamma': jnp.ones((DO,), jnp.float32), 'bn_beta': jnp.zeros((DO,), jnp.float32), 'bn_mean': jnp.zeros((DO,), jnp.float32), 'bn_var': jnp.ones((DO,), jnp.float32)}
    _L0_conv_all = _L0_conv_setup()
    _L0_conv_in = {k: v for k, v in _L0_conv_all.items() if k in ('theta_w', 'theta_b', 'phi_w', 'phi_b', 'g_w', 'g_b', 'out_w', 'out_b', 'bn_gamma', 'bn_beta', 'bn_mean', 'bn_var', )}
    del _L0_conv_all

    def _L1_conv_setup():
        import jax, jax.numpy as jnp
        import numpy as np

        def _ln(x, g, b, eps=1e-05):
            m = jnp.mean(x, -1, keepdims=True)
            xc = x - m
            v = jnp.mean(xc * xc, -1, keepdims=True)
            return xc * jax.lax.rsqrt(v + eps) * g + b

        def _ss2d(x, in_W, conv_W, conv_b, x_proj_W, dt_W, dt_b, A_logs, Ds, og, ob, out_W):
            B, H, Wd, _ = x.shape
            Di = in_W.shape[1]
            K = x_proj_W.shape[0]
            R = dt_W.shape[2]
            N = (x_proj_W.shape[1] - R) // 2
            x = x @ in_W
            x = x.transpose(0, 3, 1, 2)
            x = jax.lax.conv_general_dilated(x, conv_W, (1, 1), 'SAME', feature_group_count=Di, dimension_numbers=('NCHW', 'OIHW', 'NCHW'))
            x = jax.nn.silu(x + conv_b[None, :, None, None])
            L = H * Wd
            x0 = x.reshape(B, Di, L)
            x1 = x.transpose(0, 1, 3, 2).reshape(B, Di, L)
            xs = jnp.stack([x0, x1, x0[..., ::-1], x1[..., ::-1]], 1)
            dbl = jnp.einsum('bkdl,kcd->bkcl', xs, x_proj_W)
            dts, Bmat, Cmat = jnp.split(dbl, [R, R + N], axis=2)
            delta = jax.nn.softplus(jnp.einsum('bkrl,kdr->bkdl', dts, dt_W) + dt_b[None, :, :, None])
            A = -jnp.exp(A_logs).reshape(K, Di, N)
            d_t = delta.transpose(3, 0, 1, 2)
            u_t = xs.transpose(3, 0, 1, 2)
            B_t = Bmat.transpose(3, 0, 1, 2)
            C_t = Cmat.transpose(3, 0, 1, 2)

            def step(h, inp):
                d, u, Bv, Cv = inp
                dA = jnp.exp(d[..., None] * A)
                h = h * dA + (d * u)[..., None] * Bv[:, :, None, :]
                return (h, jnp.einsum('bkdn,bkn->bkd', h, Cv))
            h0 = jnp.zeros((B, K, Di, N), x.dtype)
            _, ys = jax.lax.scan(step, h0, (d_t, u_t, B_t, C_t))
            ys = ys.transpose(1, 2, 3, 0)
            ys = ys + xs * Ds.reshape(1, K, Di, 1)
            y = ys[:, 0] + ys[:, 2, :, ::-1]
            y2 = ys[:, 1] + ys[:, 3, :, ::-1]
            y = y + y2.reshape(B, Di, Wd, H).transpose(0, 1, 3, 2).reshape(B, Di, L)
            y = y.reshape(B, Di, H, Wd).transpose(0, 2, 3, 1)
            y = _ln(y, og, ob)
            return y @ out_W

        def _pvm(x, ln_g, ln_b, skip_scale, proj_W, proj_b, in_W, conv_W, conv_b, x_proj_W, dt_W, dt_b, A_logs, Ds, onorm_g, onorm_b, out_W):
            x = x.transpose(0, 2, 3, 1)
            xn = _ln(x, ln_g, ln_b)
            branches = jnp.split(xn, 4, axis=3)
            outs = [_ss2d(xi, in_W, conv_W, conv_b, x_proj_W, dt_W, dt_b, A_logs, Ds, onorm_g, onorm_b, out_W) + skip_scale * xi for xi in branches]
            y = jnp.concatenate(outs, -1)
            y = _ln(y, ln_g, ln_b)
            y = y @ proj_W + proj_b
            return y.transpose(0, 3, 1, 2)
        key = jax.random.key(seed)
        ks = jax.random.split(key, 16)
        B, C, H, W = (2, 256, 48, 48)
        Dm, Di, R, N, K, Co = (C // 4, C // 2, 4, 16, 4, 256)
        dt = jax.random.uniform(ks[10], (K, Di), minval=0.001, maxval=0.1)
        return {'x': jax.random.normal(ks[0], (B, C, H, W), jnp.float32), 'ln_g': jnp.ones((C,), jnp.float32), 'ln_b': jnp.zeros((C,), jnp.float32), 'skip_scale': jnp.ones((1,), jnp.float32), 'proj_W': jax.random.normal(ks[1], (C, Co), jnp.float32) * C ** (-0.5), 'proj_b': jnp.zeros((Co,), jnp.float32), 'in_W': jax.random.normal(ks[2], (Dm, Di), jnp.float32) * Dm ** (-0.5), 'conv_W': jax.random.normal(ks[3], (Di, 1, 3, 3), jnp.float32) * 0.2, 'conv_b': jax.random.normal(ks[4], (Di,), jnp.float32) * 0.02, 'x_proj_W': jax.random.normal(ks[5], (K, R + 2 * N, Di), jnp.float32) * Di ** (-0.5), 'dt_W': jax.random.normal(ks[6], (K, Di, R), jnp.float32) * R ** (-0.5), 'dt_b': dt + jnp.log(-jnp.expm1(-dt)), 'A_logs': jnp.log(jnp.tile(jnp.arange(1, N + 1, dtype=jnp.float32), (K * Di, 1))), 'Ds': jnp.ones((K * Di,), jnp.float32), 'onorm_g': jnp.ones((Di,), jnp.float32), 'onorm_b': jnp.zeros((Di,), jnp.float32), 'out_W': jax.random.normal(ks[7], (Di, Dm), jnp.float32) * Di ** (-0.5)}
    _L1_conv_all = _L1_conv_setup()
    _L1_conv_in = {k: v for k, v in _L1_conv_all.items() if k in ('ln_g', 'ln_b', 'skip_scale', 'proj_W', 'proj_b', 'in_W', 'conv_W', 'conv_b', 'x_proj_W', 'dt_W', 'dt_b', 'A_logs', 'Ds', 'onorm_g', 'onorm_b', 'out_W', )}
    del _L1_conv_all

    return {
        "x": x,
        "L0_conv_theta_w": _L0_conv_in["theta_w"],
        "L0_conv_theta_b": _L0_conv_in["theta_b"],
        "L0_conv_phi_w": _L0_conv_in["phi_w"],
        "L0_conv_phi_b": _L0_conv_in["phi_b"],
        "L0_conv_g_w": _L0_conv_in["g_w"],
        "L0_conv_g_b": _L0_conv_in["g_b"],
        "L0_conv_out_w": _L0_conv_in["out_w"],
        "L0_conv_out_b": _L0_conv_in["out_b"],
        "L0_conv_bn_gamma": _L0_conv_in["bn_gamma"],
        "L0_conv_bn_beta": _L0_conv_in["bn_beta"],
        "L0_conv_bn_mean": _L0_conv_in["bn_mean"],
        "L0_conv_bn_var": _L0_conv_in["bn_var"],
        "L1_conv_ln_g": _L1_conv_in["ln_g"],
        "L1_conv_ln_b": _L1_conv_in["ln_b"],
        "L1_conv_skip_scale": _L1_conv_in["skip_scale"],
        "L1_conv_proj_W": _L1_conv_in["proj_W"],
        "L1_conv_proj_b": _L1_conv_in["proj_b"],
        "L1_conv_in_W": _L1_conv_in["in_W"],
        "L1_conv_conv_W": _L1_conv_in["conv_W"],
        "L1_conv_conv_b": _L1_conv_in["conv_b"],
        "L1_conv_x_proj_W": _L1_conv_in["x_proj_W"],
        "L1_conv_dt_W": _L1_conv_in["dt_W"],
        "L1_conv_dt_b": _L1_conv_in["dt_b"],
        "L1_conv_A_logs": _L1_conv_in["A_logs"],
        "L1_conv_Ds": _L1_conv_in["Ds"],
        "L1_conv_onorm_g": _L1_conv_in["onorm_g"],
        "L1_conv_onorm_b": _L1_conv_in["onorm_b"],
        "L1_conv_out_W": _L1_conv_in["out_W"],
    }

def reference(x, L0_conv_theta_w, L0_conv_theta_b, L0_conv_phi_w, L0_conv_phi_b, L0_conv_g_w, L0_conv_g_b, L0_conv_out_w, L0_conv_out_b, L0_conv_bn_gamma, L0_conv_bn_beta, L0_conv_bn_mean, L0_conv_bn_var, L1_conv_ln_g, L1_conv_ln_b, L1_conv_skip_scale, L1_conv_proj_W, L1_conv_proj_b, L1_conv_in_W, L1_conv_conv_W, L1_conv_conv_b, L1_conv_x_proj_W, L1_conv_dt_W, L1_conv_dt_b, L1_conv_A_logs, L1_conv_Ds, L1_conv_onorm_g, L1_conv_onorm_b, L1_conv_out_W):
    import jax
    import jax.numpy as jnp
    def _L0_conv_ref(x, theta_w, theta_b, phi_w, phi_b, g_w, g_b, out_w, out_b, bn_gamma, bn_beta, bn_mean, bn_var):
        import jax, jax.numpy as jnp
        import numpy as np
        BN_EPS = 1e-05

        def conv1x1(x, w, b):
            return jnp.einsum('bchw,oc->bohw', x, w) + b[None, :, None, None]
        B, C, H, W = x.shape
        DI = theta_w.shape[0]
        N = H * W
        theta = conv1x1(x, theta_w, theta_b).reshape(B, DI, N)
        phi = conv1x1(x, phi_w, phi_b).reshape(B, DI, N)
        g = conv1x1(x, g_w, g_b).reshape(B, DI, N)
        scores = jnp.einsum('bdn,bdm->bnm', theta, phi) * DI ** (-0.5)
        p = jax.nn.softmax(scores, axis=-1)
        t = jnp.einsum('bdm,bnm->bdn', g, p).reshape(B, DI, H, W)
        out = conv1x1(t, out_w, out_b)
        inv = jax.lax.rsqrt(bn_var + BN_EPS)
        out = (out - bn_mean[None, :, None, None]) * (bn_gamma * inv)[None, :, None, None] + bn_beta[None, :, None, None]
        return out + x

    def _L1_conv_ref(x, ln_g, ln_b, skip_scale, proj_W, proj_b, in_W, conv_W, conv_b, x_proj_W, dt_W, dt_b, A_logs, Ds, onorm_g, onorm_b, out_W):
        import jax, jax.numpy as jnp
        import numpy as np

        def _ln(x, g, b, eps=1e-05):
            m = jnp.mean(x, -1, keepdims=True)
            xc = x - m
            v = jnp.mean(xc * xc, -1, keepdims=True)
            return xc * jax.lax.rsqrt(v + eps) * g + b

        def _ss2d(x, in_W, conv_W, conv_b, x_proj_W, dt_W, dt_b, A_logs, Ds, og, ob, out_W):
            B, H, Wd, _ = x.shape
            Di = in_W.shape[1]
            K = x_proj_W.shape[0]
            R = dt_W.shape[2]
            N = (x_proj_W.shape[1] - R) // 2
            x = x @ in_W
            x = x.transpose(0, 3, 1, 2)
            x = jax.lax.conv_general_dilated(x, conv_W, (1, 1), 'SAME', feature_group_count=Di, dimension_numbers=('NCHW', 'OIHW', 'NCHW'))
            x = jax.nn.silu(x + conv_b[None, :, None, None])
            L = H * Wd
            x0 = x.reshape(B, Di, L)
            x1 = x.transpose(0, 1, 3, 2).reshape(B, Di, L)
            xs = jnp.stack([x0, x1, x0[..., ::-1], x1[..., ::-1]], 1)
            dbl = jnp.einsum('bkdl,kcd->bkcl', xs, x_proj_W)
            dts, Bmat, Cmat = jnp.split(dbl, [R, R + N], axis=2)
            delta = jax.nn.softplus(jnp.einsum('bkrl,kdr->bkdl', dts, dt_W) + dt_b[None, :, :, None])
            A = -jnp.exp(A_logs).reshape(K, Di, N)
            d_t = delta.transpose(3, 0, 1, 2)
            u_t = xs.transpose(3, 0, 1, 2)
            B_t = Bmat.transpose(3, 0, 1, 2)
            C_t = Cmat.transpose(3, 0, 1, 2)

            def step(h, inp):
                d, u, Bv, Cv = inp
                dA = jnp.exp(d[..., None] * A)
                h = h * dA + (d * u)[..., None] * Bv[:, :, None, :]
                return (h, jnp.einsum('bkdn,bkn->bkd', h, Cv))
            h0 = jnp.zeros((B, K, Di, N), x.dtype)
            _, ys = jax.lax.scan(step, h0, (d_t, u_t, B_t, C_t))
            ys = ys.transpose(1, 2, 3, 0)
            ys = ys + xs * Ds.reshape(1, K, Di, 1)
            y = ys[:, 0] + ys[:, 2, :, ::-1]
            y2 = ys[:, 1] + ys[:, 3, :, ::-1]
            y = y + y2.reshape(B, Di, Wd, H).transpose(0, 1, 3, 2).reshape(B, Di, L)
            y = y.reshape(B, Di, H, Wd).transpose(0, 2, 3, 1)
            y = _ln(y, og, ob)
            return y @ out_W

        def _pvm(x, ln_g, ln_b, skip_scale, proj_W, proj_b, in_W, conv_W, conv_b, x_proj_W, dt_W, dt_b, A_logs, Ds, onorm_g, onorm_b, out_W):
            x = x.transpose(0, 2, 3, 1)
            xn = _ln(x, ln_g, ln_b)
            branches = jnp.split(xn, 4, axis=3)
            outs = [_ss2d(xi, in_W, conv_W, conv_b, x_proj_W, dt_W, dt_b, A_logs, Ds, onorm_g, onorm_b, out_W) + skip_scale * xi for xi in branches]
            y = jnp.concatenate(outs, -1)
            y = _ln(y, ln_g, ln_b)
            y = y @ proj_W + proj_b
            return y.transpose(0, 3, 1, 2)
        return _pvm(x, ln_g, ln_b, skip_scale, proj_W, proj_b, in_W, conv_W, conv_b, x_proj_W, dt_W, dt_b, A_logs, Ds, onorm_g, onorm_b, out_W)

    def _gn(v, G=32, eps=1e-5):
        B_, C_, H_, W_ = v.shape
        g = v.reshape(B_, G, C_ // G, H_, W_)
        m = jnp.mean(g, axis=(2, 3, 4), keepdims=True)
        s = jnp.var(g, axis=(2, 3, 4), keepdims=True)
        return ((g - m) / jnp.sqrt(s + eps)).reshape(v.shape)

    def _ln_c(v, eps=1e-6):
        m = jnp.mean(v, axis=1, keepdims=True)
        s = jnp.var(v, axis=1, keepdims=True)
        return (v - m) / jnp.sqrt(s + eps)

    def _ln_t(v, eps=1e-5):
        m = jnp.mean(v, axis=-1, keepdims=True)
        s = jnp.var(v, axis=-1, keepdims=True)
        return (v - m) / jnp.sqrt(s + eps)

    def _to_tokens(v):
        B_, C_, H_, W_ = v.shape
        return v.reshape(B_, C_, H_ * W_).transpose(0, 2, 1)
    def _from_tokens(t, like):
        B_, C_, H_, W_ = like.shape
        return t.transpose(0, 2, 1).reshape(B_, C_, H_, W_)

    x = _L0_conv_ref(x, L0_conv_theta_w, L0_conv_theta_b, L0_conv_phi_w, L0_conv_phi_b, L0_conv_g_w, L0_conv_g_b, L0_conv_out_w, L0_conv_out_b, L0_conv_bn_gamma, L0_conv_bn_beta, L0_conv_bn_mean, L0_conv_bn_var)
    x = _L1_conv_ref(x, L1_conv_ln_g, L1_conv_ln_b, L1_conv_skip_scale, L1_conv_proj_W, L1_conv_proj_b, L1_conv_in_W, L1_conv_conv_W, L1_conv_conv_b, L1_conv_x_proj_W, L1_conv_dt_W, L1_conv_dt_b, L1_conv_A_logs, L1_conv_Ds, L1_conv_onorm_g, L1_conv_onorm_b, L1_conv_out_W)
    return x


_drawn_inputs = setup_inputs


def setup_inputs(seed=0):
    import zlib

    import numpy as np

    out = dict(_drawn_inputs(seed))
    spreads = {'L0_conv_bn_gamma': (1.0, 0.6),
     'L0_conv_bn_beta': (0.0, 0.1),
     'L0_conv_bn_mean': (0.0, 0.1),
     'L0_conv_bn_var': (1.0, 0.6),
     'L1_conv_ln_g': (1.0, 0.2),
     'L1_conv_ln_b': (0.0, 0.1),
     'L1_conv_proj_b': (0.0, 0.1),
     'L1_conv_Ds': (1.0, 0.6),
     'L1_conv_onorm_g': (1.0, 0.2),
     'L1_conv_onorm_b': (0.0, 0.1)}
    factors = {'L0_conv_theta_b': 26.262,
     'L0_conv_phi_b': 64.0,
     'L0_conv_g_b': 5.685,
     'L0_conv_out_b': 5.784,
     'L1_conv_x_proj_W': 4.283,
     'L1_conv_dt_W': 8.0,
     'L1_conv_dt_b': 8.0,
     'L1_conv_A_logs': 6.561}
    for name, (base, spread) in spreads.items():
        noise = np.random.default_rng([zlib.crc32(name.encode()), seed]).standard_normal(out[name].shape)
        drawn = base * np.exp(spread * noise) if base else spread * noise
        out[name] = jnp.asarray(drawn.astype(out[name].dtype))
    for name, factor in factors.items():
        out[name] = (out[name] * factor).astype(out[name].dtype)
    return out
```

```python
from contextlib import ExitStack

import concourse.bass as bass
from concourse import mybir

F32 = mybir.dt.float32
BF16 = mybir.dt.bfloat16
ALU = mybir.AluOpType
ACT = mybir.ActivationFunctionType
AX = mybir.AxisListType.X

P = 128
B, C, H, W = 8, 256, 56, 56
L = H * W
CH = 8 * W
NC = L // CH
HP, WP = H + 2, W + 2
LP = HP * WP
DI = 128
DM = 64
BR = C // DM
K, N, R = 4, 16, 4
NT = C // P
MT = 112
NM = L // MT
UNITS = B * BR
PAIRS = N // 2
ROUNDS = K * NC
EPS = 1e-5
SMALL = 2.0 ** -9

COLS = ["theta_b", "phi_b", "g_b", "conv_b", "onorm_g", "onorm_b", "skip", "eps", "small"]
COL = {n: i for i, n in enumerate(COLS)}
NCOLS = len(COLS)
for _name, _width in (("out_b", NT), ("gamma", NT), ("beta", NT), ("mean", NT), ("var", NT), ("ln_g", NT),
                      ("ln_b", NT), ("proj_b", NT), ("dt_b", K), ("Ds", K), ("A_logs", K * N)):
    COL[_name] = NCOLS
    NCOLS += _width

TABLES = "natural_log_exp_and_others"

ORDER = [0, 2, 1, 3]


def done(rate, t, i=0):
    return t * rate + (rate + i + 1)


def build(nc, d):
    with ExitStack() as top:
        def sem(name):
            return top.enter_context(nc.semaphore(name))

        def sb(name, shape, dt=F32, scope=top):
            return scope.enter_context(nc.sbuf_tensor(name, shape, dt))

        cols = sb("cols", [P, NCOLS])
        ident = sb("ident", [P, P])
        ones = sb("ones", [P, P])
        ones_di = sb("ones_di", [P, P])
        ones_c = sb("ones_c", [P, P])
        ones3 = sb("ones3", [3, MT], BF16)
        neg_conv_b = sb("neg_conv_b", [P, 1])
        A = sb("A", [P, K * N])
        Ds_sum = sb("Ds_sum", [P, 1])
        ln_small = sb("ln_small", [P, 2])
        dt_shift = sb("dt_shift", [P, K])
        bn_scale = sb("bn_scale", [P, NT])
        bn_shift = sb("bn_shift", [P, NT])

        def col(name, i=0):
            return cols[:, COL[name] + i:COL[name] + i + 1]

        loaded = sem("loaded")
        made = sem("made")
        made_act = sem("made_act")
        made_pe = sem("made_pe")
        passed = {e: sem("passed_" + e) for e in ("pe", "act", "pool", "dve")}
        credit = {}

        def passing(eng, name):
            eng.sem_inc(passed[name], 1)

        def rated(name, rate):
            credit[name] = (sem(name), rate)
            return credit[name][0]

        w_conv = sb("w_conv", [P, 6, P])
        w_bc = sb("w_bc", [P, K, P])
        w_dt = sb("w_dt", [P, K, P])
        w_out = sb("w_out", [P, DM])
        w_proj = sb("w_proj", [P, NT, C])
        w_thph = sb("w_thph", [P, NT, 3, P])
        w_o = sb("w_o", [P, C])
        sel = sb("sel", [P, 2 * N, P], BF16)

        with ExitStack() as s:
            xp = sb("xp", [P, K, R + 2 * N], scope=s)
            xdt = sb("xdt", [R, K, P], scope=s)
            dtw = sb("dtw", [R, K, P], scope=s)
            inw = sb("inw", [P, P], scope=s)
            taps = sb("taps", [P, 6, P], scope=s)
            tmp = sb("tmp", [P, 4], scope=s)
            pw = s.enter_context(nc.psum_tensor("pw", [P, K, P], F32))

            a_load = sem("a_load")
            a_xr = sem("a_xr")
            a_nm = sem("a_nm")
            a_store = sem("a_store")
            th_mm = rated("th_mm", 1)
            ph_mm = rated("ph_mm", 1)
            th_ev = rated("th_ev", 1)
            ph_ev = rated("ph_ev", 1)
            g_mm = rated("g_mm", 7)
            g_ev = rated("g_ev", 7)
            s_mm = rated("s_mm", 7)
            s_max = rated("s_max", 7)
            mx_red = rated("mx_red", 1)
            mx_t = rated("mx_t", 1)
            nm_sp = rated("nm_sp", 5)
            st_mm = rated("st_mm", NM)
            ex = rated("ex", NM)
            av = rated("av", NM)
            acc_s = rated("acc_s", NM)
            den_mm = rated("den_mm", 1)
            rden_s = rated("rden_s", 1)
            tr_s = rated("tr_s", 1)
            t0_s = rated("t0_s", 1)
            t_s = rated("t_s", 1)
            o_mm = rated("o_mm", 1)
            y_s = rated("y_s", 1)
            x1_s = rated("x1_s", 1)
            mean_mm = rated("mean_mm", 1)
            xc_s = rated("xc_s", 1)
            sq_s = rated("sq_s", 1)
            var_mm = rated("var_mm", 1)
            ln_s = rated("ln_s", 1)
            rs_s = rated("rs_s", 1)
            xh_s = rated("xh_s", 1)
            xn_s = rated("xn_s", 1)
            c_load = sem("c_load")
            k_load = sem("k_load")
            b_store = sem("b_store")
            b_mm = rated("b_mm", PAIRS)
            b_cp = rated("b_cp", PAIRS)
            dbu_s = rated("dbu_s", PAIRS)
            e_s = rated("e_s", N)
            h_s = rated("h_s", N)
            c_mm = rated("c_mm", PAIRS)
            p_s = rated("p_s", PAIRS)
            y_mm = rated("y_mm", PAIRS)
            yev = rated("yev", 1)
            bc_mm = rated("bc_mm", 1)
            bc_f = rated("bc_f", 1)
            bc_hi = rated("bc_hi", 1)
            bc_r = rated("bc_r", 1)
            bc_mid = rated("bc_mid", 1)
            bc_lo = rated("bc_lo", 1)
            dt_mm = rated("dt_mm", 1)
            dt_x = rated("dt_x", 1)
            dt_abs = rated("dt_abs", 1)
            dt_relu = rated("dt_relu", 1)
            dt_e = rated("dt_e", 1)
            dt_c = rated("dt_c", 2)
            dt_s = rated("dt_s", 2)
            dt_p = rated("dt_p", 1)
            dt_d = rated("dt_d", 1)
            dt_u = rated("dt_u", 1)
            cv_mm = rated("cv_mm", 1)
            cv_u = rated("cv_u", 1)
            cv_e = rated("cv_e", 1)
            cv_l = rated("cv_l", 1)
            cv_s = rated("cv_s", 1)
            x_s = rated("x_s", 1)
            xt_s = rated("xt_s", 1)
            h_zero = rated("h_zero", K)
            l_mean = rated("l_mean", 1)
            l_yc = rated("l_yc", 1)
            l_sq = rated("l_sq", 1)
            l_var = rated("l_var", 1)
            l_ln = rated("l_ln", 1)
            l_rs = rated("l_rs", 1)
            l_yn = rated("l_yn", 1)
            l_yg = rated("l_yg", 1)
            l_out = rated("l_out", 1)
            l_bo = rated("l_bo", 1)
            zeroed = sem("zeroed")
            f_load = [sem("f_load0"), sem("f_load1")]
            f_store = [sem("f_store0"), sem("f_store1")]
            f_mean = rated("f_mean", 1)
            f_cen = rated("f_cen", 1)
            f_sqr = rated("f_sqr", 1)
            f_var = rated("f_var", 1)
            f_ln = rated("f_ln", 1)
            f_rsd = rated("f_rsd", 1)
            f_nrm = rated("f_nrm", 1)
            f_aff = rated("f_aff", 1)
            f_mm = rated("f_mm", 1)
            f_oa = rated("f_oa", 1)
            f_ov = rated("f_ov", 1)

            block = s.enter_context(nc.Block())

            @block.sync
            def _(sp):
                for dst, src in ((cols[:], d["cols"]), (ident[:], d["ident"]), (sel[:], d["sel"]),
                                 (xp[:], d["xp"]), (xdt[:], d["xdt"]), (dtw[:], d["dtw"]),
                                 (inw[:], d["inw2"]), (taps[:], d["taps"]), (w_out[:], d["out_W"]),
                                 (w_proj[:], d["proj_W"].rearrange("(t p) o -> p t o", p=P)),
                                 (w_thph[:], d["thph"].rearrange("(t p) a o -> p t a o", p=P)),
                                 (w_o[:], d["w_o"])):
                    sp.dma_start(dst, src).then_inc(loaded, 16)

            @block.gpsimd
            def _(pool):
                pool.memset(ones[:], 1.0)
                pool.memset(ones_di[:], 1.0 / DI)
                pool.memset(ones_c[:], 1.0 / C)
                pool.memset(ones3[:], 1.0)
                for s_, rate in credit.values():
                    pool.sem_inc(s_, rate)

            @block.tensor
            def _(pe):
                pe.wait_ge(loaded, 16 * 12)
                for k in range(K):
                    mm = pe.matmul(pw[:, k, :], xdt[:, k, :], dtw[:, k, :], start=True, stop=True)
                mm.then_inc(made_pe, 1)

            @block.scalar
            def _(act):
                act.preload_act_table_set(TABLES)
                act.wait_ge(loaded, 16 * 12)
                act.activation(A[:], cols[:, COL["A_logs"]:COL["A_logs"] + K * N], ACT.Exp)\
                   .then_inc(made_act, 1)
                act.activation(tmp[:, 0:NT], cols[:, COL["var"]:COL["var"] + NT], ACT.Ln, bias=col("eps"))\
                   .then_inc(made_act, 1)
                act.activation(ln_small[:, 0:1], col("small"), ACT.Ln, bias=1.0).then_inc(made_act, 1)
                act.wait_ge(made_act, 3)
                act.activation(tmp[:, 2:2 + NT], tmp[:, 0:NT], ACT.Exp, scale=-0.5).then_inc(made_act, 1)

            @block.vector
            def _(dve):
                step = [0]

                def chained(ins):
                    step[0] += 1
                    ins.then_inc(made, 1)
                    dve.wait_ge(made, step[0])

                chained(dve.memset(w_bc[:], 0.0))
                dve.wait_ge(loaded, 16 * 12)
                for q in (0, 64, 96):
                    dve.tensor_copy(w_bc[:, :, q:q + 2 * N], xp[:, :, R:])
                for j in range(6):
                    dve.tensor_tensor(w_conv[:, j, :], inw[:], taps[:, j, :], ALU.mult)
                dve.tensor_scalar(neg_conv_b[:], col("conv_b"), -1.0, None, ALU.mult)
                chained(dve.tensor_reduce(Ds_sum[:], cols[:, COL["Ds"]:COL["Ds"] + K], AX, ALU.add))
                dve.wait_ge(made_act, 4)
                chained(dve.tensor_scalar(ln_small[:, 1:2], ln_small[:, 0:1], -1.0, None, ALU.mult))
                dve.tensor_scalar(dt_shift[:], cols[:, COL["dt_b"]:COL["dt_b"] + K], ln_small[:, 0:1], None,
                                  ALU.subtract)
                chained(dve.tensor_scalar(A[:], A[:], -1.0, None, ALU.mult))
                g0, b0, m0, o0 = (COL[n] for n in ("gamma", "beta", "mean", "out_b"))
                chained(dve.tensor_tensor(bn_scale[:], cols[:, g0:g0 + NT], tmp[:, 2:2 + NT], ALU.mult))
                chained(dve.tensor_tensor(bn_shift[:], cols[:, o0:o0 + NT], cols[:, m0:m0 + NT], ALU.subtract))
                chained(dve.tensor_tensor(bn_shift[:], bn_shift[:], bn_scale[:], ALU.mult))
                chained(dve.tensor_tensor(bn_shift[:], bn_shift[:], cols[:, b0:b0 + NT], ALU.add))
                dve.wait_ge(made_pe, 1)
                chained(dve.tensor_copy(w_dt[:], pw[:]))

        with ExitStack() as s:
            xg = sb("xg", [P, NT, L], scope=s)
            xr = sb("xr", [P, NT, CH], scope=s)
            th = sb("th", [P, L], scope=s)
            ph = sb("ph", [P, L], scope=s)
            gT = sb("gT", [MT, NM, P], scope=s)
            mx = sb("mx", [MT, NC, NM], scope=s)
            mxr = sb("mxr", [MT, NM], scope=s)
            nh = sb("nh", [NM, 3, MT], BF16, scope=s)
            nr = sb("nr", [NM, 2, MT], scope=s)
            nrow = sb("nrow", [3, L], BF16, scope=s)
            pex = sb("pex", [MT, 4, CH], scope=s)
            acc = sb("acc", [MT, CH], scope=s)
            rden = sb("rden", [P, CH], scope=s)
            tr = sb("tr", [P, CH], scope=s)
            t0 = sb("t0", [P, CH], scope=s)
            tt = sb("tt", [P, CH], scope=s)
            x1 = sb("x1", [P, NT, CH], scope=s)
            xc = sb("xc", [P, NT, CH], scope=s)
            sq = sb("sq", [P, NT, CH], scope=s)
            rs = sb("rs", [P, CH], scope=s)
            xh = sb("xh", [P, NT, CH], scope=s)
            xnp = sb("xnp", [P, NT, HP, WP], scope=s)
            pp = s.enter_context(nc.psum_tensor("pp", [P, 8, 512], F32))
            T, M0, M1, M2 = (pp[:, i, 0:CH] for i in (4, 5, 6, 7))
            block = s.enter_context(nc.Block())
            scale = float(DI) ** -0.5

            @block.sync
            def _(sp):
                def load_x(b):
                    sp.dma_start(xg[:], d["x"][bass.ds(b, 1)].rearrange("a (t p) l -> p (a t) l", p=P))\
                      .then_inc(a_load, 16)

                load_x(0)
                with sp.Fori(0, B) as b:
                    sp.wait_ge(g_mm, done(7, b, 6))
                    load_x((b + 1) % B)
                    sp.wait_ge(nm_sp, done(5, b, 4))
                    for i in range(3):
                        sp.dma_start(nrow[i:i + 1, :], nh[:, i, :]).then_inc(a_nm, 16)
                    with sp.Fori(0, NC) as c:
                        g = b * NC + c
                        sp.wait_ge(x1_s, done(1, g - 1))
                        sp.dma_start(xr[:], d["x"][bass.ds(b, 1), :, bass.ds(c * CH, CH)]
                                     .rearrange("a (t p) l -> p (a t) l", p=P)).then_inc(a_xr, 16)
                    sp.wait_ge(xn_s, done(1, b * NC + (NC - 1)))
                    sp.dma_start(d["xn"][bass.ds(b * C, C)].rearrange("(t p) l -> p t l", p=P),
                                 xnp[:].rearrange("p t h w -> p t (h w)")).then_inc(a_store, 16)
                sp.wait_ge(a_store, 16 * B)
                sp.wait_ge(a_load, 16 * (B + 1))

            @block.tensor
            def _(pe):
                def scores_t(b, c, m):
                    pe.wait_ge(ex, done(NM, b * NC + c, m - 4))
                    pe.matmul(pp[0:MT, m % 4, 0:CH], ph[:, m * MT:(m + 1) * MT], th[:, bass.ds(c * CH, CH)],
                              start=True, stop=False)
                    pe.matmul(pp[0:MT, m % 4, 0:CH], ones3[:], nrow[:, bass.ds(c * CH, CH)],
                              start=False, stop=True).then_inc(st_mm, 1)

                def weigh(g, m):
                    pe.wait_ge(ex, done(NM, g, m))
                    if m == 0:
                        pe.wait_ge(tr_s, done(1, g - 1))
                    pe.matmul(T, gT[:, m, :], pex[:, m % 4, :], start=(m == 0), stop=(m == NM - 1))\
                      .then_inc(av, 1)

                def chain(g, step):
                    if step == 0:
                        pe.wait_ge(acc_s, done(NM, g, NM - 1))
                        pe.matmul(M0, ones[0:MT, :], acc[:], start=True, stop=True).then_inc(den_mm, 1)
                    if step == 4:
                        pe.wait_ge(t_s, done(1, g))
                        pe.wait_ge(ln_s, done(1, g - 1))
                        pe.matmul(M1, w_o[:, 0:P], tt[:], start=True, stop=True)
                        pe.matmul(M2, w_o[:, P:C], tt[:], start=True, stop=True).then_inc(o_mm, 1)
                    if step == 8:
                        pe.wait_ge(x1_s, done(1, g))
                        pe.matmul(M0, ones_c[:], x1[:, 0, :], start=True, stop=False)
                        pe.matmul(M0, ones_c[:], x1[:, 1, :], start=False, stop=True).then_inc(mean_mm, 1)
                    if step == 11:
                        pe.wait_ge(sq_s, done(1, g))
                        pe.matmul(M1, ones_c[:], sq[:, 0, :], start=True, stop=False)
                        pe.matmul(M1, ones_c[:], sq[:, 1, :], start=False, stop=True).then_inc(var_mm, 1)

                def chunk(b, c, chained):
                    g = b * NC + c
                    for m in range(NM + 2):
                        if m < NM:
                            scores_t(b, c, m)
                        if chained:
                            chain(g - 1, m)
                        if m >= 2:
                            weigh(g, m - 2)

                with pe.Fori(0, B) as b:
                    pe.wait_ge(a_load, 16 * b + 16)
                    passing(pe, "pe")
                    with pe.Fori(0, NC) as c:
                        g = b * NC + c
                        pe.wait_ge(th_ev, done(1, g - 1))
                        for t in range(NT):
                            mm = pe.matmul(pp[:, 0, 0:CH], w_thph[:, t, 0, :], xg[:, t, bass.ds(c * CH, CH)],
                                           start=(t == 0), stop=(t == NT - 1))
                        mm.then_inc(th_mm, 1)
                        pe.wait_ge(ph_ev, done(1, g - 1))
                        for t in range(NT):
                            mm = pe.matmul(pp[:, 1, 0:CH], w_thph[:, t, 1, :], xg[:, t, bass.ds(c * CH, CH)],
                                           start=(t == 0), stop=(t == NT - 1))
                        mm.then_inc(ph_mm, 1)
                    for j in range(7):
                        pe.wait_ge(g_ev, done(7, b, j - 2))
                        for i in range(4):
                            m = 4 * j + i
                            for t in range(NT):
                                mm = pe.matmul(pp[0:MT, 2 + j % 2, i * P:(i + 1) * P],
                                               xg[:, t, m * MT:(m + 1) * MT], w_thph[:, t, 2, :],
                                               start=(t == 0), stop=(t == NT - 1))
                        mm.then_inc(g_mm, 1)
                    pe.wait_ge(th_ev, done(1, b * NC + (NC - 1)))
                    pe.wait_ge(ph_ev, done(1, b * NC + (NC - 1)))
                    pe.wait_ge(g_ev, done(7, b, 6))
                    pe.wait_ge(xc_s, done(1, b * NC - 1))
                    pe.wait_ge(ln_s, done(1, b * NC - 1))
                    passing(pe, "pe")
                    def scores(c, odd):
                        for j in range(7):
                            bank = 4 * ((j + odd) % 2)
                            pe.wait_ge(s_max, done(7, b * NC + c, j - 2))
                            for i in range(4):
                                n = 4 * j + i
                                mm = pe.matmul(pp[0:MT, bank + i, 0:CH], th[:, n * MT:(n + 1) * MT],
                                               ph[:, bass.ds(c * CH, CH)], start=True, stop=True)
                            mm.then_inc(s_mm, 1)

                    with pe.Fori(0, NC // 2) as c2:
                        for odd in (0, 1):
                            scores(c2 * 2 + odd, odd)
                    scores(NC - 1, 0)
                    pe.wait_ge(mx_red, done(1, b))
                    pe.matmul(pp[0:NM, 5, 0:MT], mxr[:], ident[0:MT, 0:MT], start=True, stop=True)\
                      .then_inc(mx_t, 1)
                    pe.wait_ge(a_nm, 48 * b + 48)
                    chunk(b, 0, False)
                    with pe.Fori(1, NC) as c:
                        chunk(b, c, True)
                    for step in range(NM):
                        chain(b * NC + (NC - 1), step)

            @block.scalar
            def _(act):
                act.preload_act_table_set(TABLES)
                def chain(g, c, step):
                    if step == 3:
                        act.wait_ge(t0_s, done(1, g))
                        act.activation(tt[:], t0[:], ACT.Identity, bias=col("g_b")).then_inc(t_s, 1)
                    if step == 5:
                        act.wait_ge(o_mm, done(1, g))
                        act.wait_ge(mean_mm, done(1, g - 1))
                        act.activation(x1[:, 0, :], M1, ACT.Identity, bias=bn_shift[:, 0:1], scale=bn_scale[:, 0:1])
                        act.activation(x1[:, 1, :], M2, ACT.Identity, bias=bn_shift[:, 1:2], scale=bn_scale[:, 1:2])\
                           .then_inc(y_s, 1)
                    if step == 10:
                        act.wait_ge(xc_s, done(1, g))
                        act.activation(sq[:], xc[:], ACT.Square).then_inc(sq_s, 1)
                    if step == 12:
                        act.wait_ge(var_mm, done(1, g))
                        act.activation(rs[:], M1, ACT.Ln, bias=col("eps")).then_inc(ln_s, 1)
                        act.wait_ge(ln_s, done(1, g))
                        act.activation(rs[:], rs[:], ACT.Exp, scale=-0.5).then_inc(rs_s, 1)
                    if step == 15:
                        act.wait_ge(xh_s, done(1, g))
                        passing(act, "act")
                        for t in range(NT):
                            ins = act.activation(xnp[:, t, bass.ds(c * 8 + 1, 8), 1:1 + W],
                                                 xh[:, t, :].rearrange("p (h w) -> p h w", w=W), ACT.Identity,
                                                 bias=col("ln_b", t), scale=col("ln_g", t))
                        ins.then_inc(xn_s, 1)

                def chunk(b, c, chained):
                    g = b * NC + c
                    for m in range(NM):
                        act.wait_ge(st_mm, done(NM, g, m))
                        act.wait_ge(av, done(NM, g, m - 4))
                        act.wait_ge(acc_s, done(NM, g, m - 4))
                        act.activation(pex[:, m % 4, :], pp[0:MT, m % 4, 0:CH], ACT.Exp, scale=scale)\
                           .then_inc(ex, 1)
                        if chained:
                            chain(g - 1, c - 1, m)

                act.wait_ge(zeroed, 1)
                with act.Fori(0, B) as b:
                    with act.Fori(0, NC) as c:
                        act.wait_ge(th_mm, done(1, b * NC + c))
                        passing(act, "act")
                        act.activation(th[:, bass.ds(c * CH, CH)], pp[:, 0, 0:CH], ACT.Identity,
                                       bias=col("theta_b")).then_inc(th_ev, 1)
                    for j in range(7):
                        act.wait_ge(g_mm, done(7, b, j))
                        act.copy(gT[:, 4 * j:4 * j + 4, :],
                                 pp[0:MT, 2 + j % 2, :].rearrange("p (a n) -> p a n", a=4)).then_inc(g_ev, 1)
                    act.wait_ge(a_store, 16 * b)
                    chunk(b, 0, False)
                    with act.Fori(1, NC) as c:
                        chunk(b, c, True)
                    for step in range(NM):
                        chain(b * NC + (NC - 1), NC - 1, step)

            @block.gpsimd
            def _(pool):
                with pool.Fori(0, B * NC) as g:
                    pool.wait_ge(rs_s, done(1, g))
                    pool.wait_ge(xn_s, done(1, g - 1))
                    for t in range(NT):
                        ins = pool.tensor_tensor(xh[:, t, :], xc[:, t, :], rs[:], ALU.mult)
                    ins.then_inc(xh_s, 1)

            @block.vector
            def _(dve):
                dve.memset(xnp[:].rearrange("p t h w -> p (t h w)"), 0.0).then_inc(zeroed, 1)

                def chain(g, step):
                    if step == 0:
                        dve.wait_ge(av, done(NM, g, NM - 1))
                        dve.tensor_copy(tr[:], T).then_inc(tr_s, 1)
                    if step == 1:
                        dve.wait_ge(den_mm, done(1, g))
                        dve.reciprocal(rden[:], M0).then_inc(rden_s, 1)
                        dve.wait_ge(rden_s, done(1, g))
                        dve.wait_ge(tr_s, done(1, g))
                        dve.tensor_tensor(t0[:], tr[:], rden[:], ALU.mult).then_inc(t0_s, 1)
                    if step == 6:
                        dve.wait_ge(y_s, done(1, g))
                        dve.wait_ge(a_xr, 16 * g + 16)
                        dve.tensor_tensor(x1[:], x1[:], xr[:], ALU.add).then_inc(x1_s, 1)
                    if step == 9:
                        dve.wait_ge(mean_mm, done(1, g))
                        dve.wait_ge(xh_s, done(1, g - 1))
                        for t in range(NT):
                            ins = dve.tensor_tensor(xc[:, t, :], x1[:, t, :], M0, ALU.subtract)
                        ins.then_inc(xc_s, 1)

                def chunk(b, c, chained):
                    g = b * NC + c
                    for m in range(NM):
                        dve.wait_ge(ex, done(NM, g, m))
                        if m == 0:
                            dve.wait_ge(den_mm, done(1, g - 1))
                            dve.tensor_copy(acc[:], pex[:, 0, :]).then_inc(acc_s, 1)
                        else:
                            dve.wait_ge(acc_s, done(NM, g, m - 1))
                            dve.tensor_tensor(acc[:], acc[:], pex[:, m % 4, :], ALU.add).then_inc(acc_s, 1)
                        if chained:
                            chain(g - 1, m)

                with dve.Fori(0, B) as b:
                    with dve.Fori(0, NC) as c:
                        dve.wait_ge(ph_mm, done(1, b * NC + c))
                        dve.tensor_scalar(ph[:, bass.ds(c * CH, CH)], pp[:, 1, 0:CH], col("phi_b"), None,
                                          ALU.add).then_inc(ph_ev, 1)
                    def maxima(c, odd):
                        for j in range(7):
                            dve.wait_ge(s_mm, done(7, b * NC + c, j))
                            bank = 4 * ((j + odd) % 2)
                            dve.tensor_reduce(mx[:, bass.ds(c, 1), 4 * j:4 * j + 4].rearrange("p a n -> p (a n)"),
                                              pp[0:MT, bank:bank + 4, 0:CH], AX, ALU.max).then_inc(s_max, 1)

                    with dve.Fori(0, NC // 2) as c2:
                        for odd in (0, 1):
                            maxima(c2 * 2 + odd, odd)
                    maxima(NC - 1, 0)
                    dve.wait_ge(s_max, done(7, b * NC + (NC - 1), 6))
                    dve.tensor_reduce(mxr[:], mx[:].rearrange("p c n -> p n c"), AX, ALU.max).then_inc(mx_red, 1)
                    dve.wait_ge(mx_t, done(1, b))
                    dve.wait_ge(a_nm, 48 * b)
                    mt = pp[0:NM, 5, 0:MT]
                    dve.tensor_scalar(nh[:, 0, :], mt, -1.0, None, ALU.mult).then_inc(nm_sp, 1)
                    dve.wait_ge(nm_sp, done(5, b, 0))
                    dve.scalar_tensor_tensor(nr[:, 0, :], mt, -1.0, nh[:, 0, :], ALU.mult, ALU.subtract)\
                       .then_inc(nm_sp, 1)
                    dve.wait_ge(nm_sp, done(5, b, 1))
                    dve.tensor_copy(nh[:, 1, :], nr[:, 0, :]).then_inc(nm_sp, 1)
                    dve.wait_ge(nm_sp, done(5, b, 2))
                    dve.tensor_tensor(nr[:, 1, :], nr[:, 0, :], nh[:, 1, :], ALU.subtract).then_inc(nm_sp, 1)
                    dve.wait_ge(nm_sp, done(5, b, 3))
                    dve.tensor_copy(nh[:, 2, :], nr[:, 1, :]).then_inc(nm_sp, 1)
                    chunk(b, 0, False)
                    with dve.Fori(1, NC) as c:
                        chunk(b, c, True)
                    for step in range(NM):
                        chain(b * NC + (NC - 1), step)

        with ExitStack() as s:
            xc_pad = sb("xc_pad", [P, LP], scope=s)
            xs_pad = sb("xs_pad", [DM, LP], scope=s)
            xN = sb("xN", [P, L], scope=s)
            xT = sb("xT", [P, L], scope=s)
            ya = sb("ya", [P, L], scope=s)
            h = sb("h", [P, N, CH], scope=s)
            bc3 = sb("bc3", [P, 2, CH], BF16, scope=s)
            bcr = sb("bcr", [P, CH], scope=s)
            dl = sb("dl", [P, 2, CH], scope=s)
            du = sb("du", [P, 2, CH], scope=s)
            da = sb("da", [P, CH], scope=s)
            dr = sb("dr", [P, CH], scope=s)
            dq = sb("dq", [P, CH], scope=s)
            dw = sb("dw", [P, CH], scope=s)
            bs = sb("bs", [P, 4, 2, CH], scope=s)
            dbu = sb("dbu", [P, 4, 2, CH], scope=s)
            ex = sb("ex", [P, 4, CH], scope=s)
            prod = sb("prod", [P, 2, 2, CH], scope=s)
            sg = sb("sg", [P, L], scope=s)
            yc = sb("yc", [P, L], scope=s)
            ysq = sb("ysq", [P, CH], scope=s)
            yrs = sb("yrs", [P, CH], scope=s)
            yg = ysq
            bo = sb("bo", [DM, 2, CH], scope=s)
            b_ps = s.enter_context(nc.psum_tensor("b_ps", [P, 2, 512], F32))
            c_ps = s.enter_context(nc.psum_tensor("c_ps", [P, 2, 2, 512], F32))
            y_ps = s.enter_context(nc.psum_tensor("y_ps", [P, 512], F32))
            m_ps = s.enter_context(nc.psum_tensor("m_ps", [P, 512], F32))
            Y, M = y_ps[:, 0:CH], m_ps[:, 0:CH]
            block = s.enter_context(nc.Block())

            def natural(q, c):
                return c if q in (0, 1) else NC - 1 - c

            def source(q, c):
                return (xN if q in (0, 2) else xT)[:, bass.ds(natural(q, c) * CH, CH)]

            def sections(eng, body):
                with eng.Fori(0, UNITS) as u:
                    for i, q in enumerate(ORDER):
                        with eng.Fori(0, NC // 2) as c2:
                            for a in (0, 1):
                                c = c2 * 2 + a
                                body(u, u * ROUNDS + c + i * NC, (i * NC + a) % 2, q, c, q, c + 1, i)
                        body(u, u * ROUNDS + (i + 1) * NC - 1, (i * NC + NC - 1) % 2, q, NC - 1,
                             ORDER[(i + 1) % K], 0, i)

            @block.sync
            def _(sp):
                def load_conv(u):
                    src = d["xn"][bass.ds(u * DM, DM)]
                    sp.dma_start(xc_pad[0:DM, :], src).then_inc(c_load, 16)
                    sp.dma_start(xc_pad[DM:P, 0:LP - 1], src[:, 1:LP]).then_inc(c_load, 16)

                def store_tail(u):
                    for c in range(NC):
                        sp.wait_ge(l_bo, done(1, u * NC + c))
                        sp.dma_start(d["bo"][bass.ds(u * DM, DM), c * CH:(c + 1) * CH], bo[:, c % 2, :])\
                          .then_inc(b_store, 16)

                load_conv(0)
                sp.wait_ge(cv_mm, done(1, NC - 1))
                load_conv(1)
                with sp.Fori(0, UNITS) as u:
                    sp.dma_start(xs_pad[:], d["xn"][bass.ds(((u + (UNITS - 1)) % UNITS) * DM, DM)])\
                      .then_inc(k_load, 16)
                    sp.wait_ge(cv_mm, done(1, (u + 1) * NC + (NC - 1)))
                    load_conv((u + 2) % UNITS)
                    store_tail(u)
                sp.dma_start(xs_pad[:], d["xn"][(UNITS - 1) * DM:UNITS * DM]).then_inc(k_load, 16)
                store_tail(UNITS)
                sp.wait_ge(b_store, 16 * NC * (UNITS + 1))
                sp.wait_ge(c_load, 32 * (UNITS + 2))

            @block.tensor
            def _(pe):
                def b_pair(t, s, par):
                    pe.wait_ge(b_cp, done(8, t, s - 1))
                    n = 2 * (s % 8)
                    pe.matmul(b_ps[:, 0, 0:CH], sel[:, n, :], bc3[:, par, :], start=True, stop=True)
                    pe.matmul(b_ps[:, 1, 0:CH], sel[:, n + 1, :], bc3[:, par, :], start=True, stop=True)\
                      .then_inc(b_mm, 1)

                def c_pair(t, s, par):
                    pe.wait_ge(p_s, done(8, t, s - 2))
                    n = N + 2 * (s % 8)
                    pe.matmul(c_ps[:, s % 2, 0, 0:CH], sel[:, n, :], bc3[:, par, :], start=True, stop=True)
                    pe.matmul(c_ps[:, s % 2, 1, 0:CH], sel[:, n + 1, :], bc3[:, par, :], start=True, stop=True)\
                      .then_inc(c_mm, 1)

                def y_sum(t, s):
                    pe.wait_ge(p_s, done(8, t, s))
                    if s == 0:
                        pe.wait_ge(yev, done(1, t - 1))
                    for i in (0, 1):
                        mm = pe.matmul(Y, ident[:], prod[:, s % 2, i, :], start=(s == 0 and i == 0),
                                       stop=(s == PAIRS - 1 and i == 1))
                    mm.then_inc(y_mm, 1)

                def prep_bc(t, q, c):
                    pe.wait_ge(dt_x, done(1, t - 1))
                    pe.matmul(M, w_bc[:, q, :], source(q, c), start=True, stop=True).then_inc(bc_mm, 1)

                def prep_dt(t, q, c):
                    pe.wait_ge(bc_f, done(1, t))
                    pe.matmul(M, w_dt[:, q, :], source(q, c), start=True, stop=True).then_inc(dt_mm, 1)

                def m_free(t):
                    if t is not None:
                        pe.wait_ge(dt_x, done(1, t))

                def conv(v, c, part, t=None):
                    rows = xc_pad[:].rearrange("p (h w) -> p h w", w=WP)
                    for j in part:
                        if j == 0:
                            m_free(t)
                            pe.wait_ge(cv_e, done(1, v - 1))
                        dy, dx = j % 3, 0 if j < 3 else 2
                        mm = pe.matmul(M, w_conv[:, j, :], rows[:, bass.ds(c * 8 + dy, 8), dx:dx + W],
                                       start=(j == 0), stop=(j == 5))
                        if j == 5:
                            mm.then_inc(cv_mm, 1)

                def tail_mean(v, c, t=None):
                    m_free(t)
                    pe.wait_ge(l_yc, done(1, v - 1))
                    pe.matmul(M, ones_di[:], ya[:, bass.ds(c * CH, CH)], start=True, stop=True)\
                      .then_inc(l_mean, 1)

                def tail_var(v, t=None):
                    m_free(t)
                    pe.wait_ge(l_ln, done(1, v - 1))
                    pe.wait_ge(l_sq, done(1, v))
                    pe.matmul(M, ones_di[:], ysq[:], start=True, stop=True).then_inc(l_var, 1)

                def tail_out(v, t=None):
                    m_free(t)
                    pe.wait_ge(l_bo, done(1, v - 1))
                    pe.wait_ge(l_yg, done(1, v))
                    pe.matmul(m_ps[0:DM, 0:CH], w_out[:], yg[:], start=True, stop=True).then_inc(l_out, 1)

                def body(u, t, par, q, c, nq, n_c, sec):
                    last = isinstance(c, int)
                    v, v1 = u * NC, (u + 1) * NC
                    for s in range(1, 9):
                        if s == 6:
                            pe.wait_ge(bc_lo, done(1, t + 1))
                        b_pair(t, s + 2, par if s < 6 else 1 - par)
                        c_pair(t, s, par if s < 8 else 1 - par)
                        if s > 1:
                            y_sum(t, s - 2)
                        if s == 8:
                            y_sum(t, 7)
                        if s == 1:
                            if sec == 0:
                                pe.wait_ge(l_yc, done(1, v + c - 1))
                                pe.wait_ge(l_bo, done(1, v - 1))
                                pe.wait_ge(x_s, done(1, v + (NC - 1)))
                            if sec == 1:
                                pe.wait_ge(l_ln, done(1, v + c - 1))
                                pe.wait_ge(l_yc, done(1, v + (NC - 1)))
                                if last:
                                    pe.wait_ge(xt_s, done(1, v + (NC - 2)))
                            if sec == 2:
                                pe.wait_ge(cv_e, done(1, v1 + c - 1))
                                pe.wait_ge(l_ln, done(1, v + (NC - 1)))
                                pe.wait_ge(xt_s, done(1, v + (NC - 1)))
                            if sec == 3:
                                pe.wait_ge(l_bo, done(1, v + c - 1))
                                pe.wait_ge(cv_e, done(1, v1 + (NC - 1)))
                                if last:
                                    pe.wait_ge(x_s, done(1, v1 + (NC - 2)))
                            prep_bc(t + 1, nq, n_c)
                        if s == 2:
                            prep_dt(t + 1, nq, n_c)
                        if s == 5 and sec == 0:
                            tail_mean(v + c, c, t + 1)
                        if s == 5 and sec == 1:
                            tail_var(v + c, t + 1)
                        if s == 5 and sec == 3:
                            tail_out(v + c, t + 1)
                        if s in (5, 6, 7) and sec == 2:
                            conv(v1 + c, c, (2 * (s - 5), 2 * (s - 5) + 1), t + 1)

                pe.wait_ge(c_load, 32)
                pe.wait_ge(zeroed, 2)
                with pe.Fori(0, NC) as c:
                    conv(c, c, range(6))
                pe.wait_ge(cv_e, done(1, NC - 1))
                pe.wait_ge(x_s, done(1, NC - 1))
                prep_bc(0, ORDER[0], 0)
                prep_dt(0, ORDER[0], 0)
                pe.wait_ge(bc_lo, done(1, 0))
                b_pair(-1, 8, 0)
                b_pair(-1, 9, 0)
                b_pair(-1, 10, 0)
                c_pair(-1, 8, 0)
                with pe.Fori(0, UNITS) as u:
                    for i, q in enumerate(ORDER):
                        if i == 2:
                            pe.wait_ge(c_load, 32 * u + 64)
                            passing(pe, "pe")
                        with pe.Fori(0, NC // 2) as c2:
                            for a in (0, 1):
                                c = c2 * 2 + a
                                body(u, u * ROUNDS + c + i * NC, (i * NC + a) % 2, q, c, q, c + 1, i)
                        body(u, u * ROUNDS + ((i + 1) * NC - 1), (i * NC + NC - 1) % 2, q, NC - 1,
                             ORDER[(i + 1) % K], 0, i)
                pe.wait_ge(yev, done(1, UNITS * ROUNDS - 1))
                with pe.Fori(0, NC) as c:
                    tail_mean(c + UNITS * NC, c)
                pe.wait_ge(l_yc, done(1, UNITS * NC + (NC - 1)))
                with pe.Fori(0, NC) as c:
                    tail_var(c + UNITS * NC)
                pe.wait_ge(l_ln, done(1, UNITS * NC + (NC - 1)))
                with pe.Fori(0, NC) as c:
                    tail_out(c + UNITS * NC)

            @block.scalar
            def _(act):
                act.preload_act_table_set(TABLES)
                def b_copy(t, s):
                    act.wait_ge(b_mm, done(8, t, s))
                    act.wait_ge(dbu_s, done(8, t, s - 4))
                    act.copy(bs[:, s % 4, :, :], b_ps[:, :, 0:CH]).then_inc(b_cp, 1)

                def decay(t, s, q, par):
                    for i in (0, 1):
                        n = 2 * (s % 8) + i
                        act.wait_ge(h_s, done(16, t, 2 * s + i - 4))
                        act.activation(ex[:, n % 4, :], dl[:, par, :], ACT.Exp,
                                       scale=A[:, q * N + n:q * N + n + 1]).then_inc(e_s, 1)

                def prep(t, q, par, s):
                    if s == 2:
                        act.wait_ge(bc_mm, done(1, t))
                        act.copy(bcr[:], M).then_inc(bc_f, 1)
                        act.wait_ge(c_mm, done(8, t - 2, 7))
                        act.wait_ge(bc_f, done(1, t))
                        act.copy(bc3[:, par, :], bcr[:]).then_inc(bc_hi, 1)
                    if s == 3:
                        act.wait_ge(dt_mm, done(1, t))
                        act.activation(da[:], M, ACT.Abs, bias=col("dt_b", q)).then_inc(dt_abs, 1)
                        act.activation(dr[:], M, ACT.Identity, bias=dt_shift[:, q:q + 1]).then_inc(dt_x, 1)
                        act.wait_ge(dt_abs, done(1, t))
                        act.activation(da[:], da[:], ACT.Exp, scale=-1.0).then_inc(dt_e, 1)
                    if s == 4:
                        act.wait_ge(bc_r, done(1, t))
                        act.copy(bc3[64:P, par, :], bcr[64:P, :]).then_inc(bc_mid, 1)
                    if s == 5:
                        act.wait_ge(dt_c, done(2, t, 1))
                        act.activation(da[:], dw[:], ACT.Exp, scale=-0.5).then_inc(dt_s, 1)
                        act.activation(dq[:], dq[:], ACT.Ln, bias=1.0).then_inc(dt_s, 1)

                def conv(v, c):
                    at = bass.ds(c * CH, CH)
                    act.wait_ge(cv_mm, done(1, v))
                    passing(act, "act")
                    act.activation(xN[:, at], M, ACT.Identity, bias=col("conv_b")).then_inc(cv_u, 1)
                    act.activation(sg[:, at], M, ACT.Exp, bias=neg_conv_b[:], scale=-1.0).then_inc(cv_e, 1)
                    act.wait_ge(cv_e, done(1, v))
                    passing(act, "act")
                    act.activation(sg[:, at], sg[:, at], ACT.Ln, bias=1.0).then_inc(cv_l, 1)
                    act.wait_ge(cv_l, done(1, v))
                    passing(act, "act")
                    act.activation(sg[:, at], sg[:, at], ACT.Exp, scale=-1.0).then_inc(cv_s, 1)

                def tail_sq(v0, c):
                    v = v0 + c
                    act.wait_ge(l_yc, done(1, v))
                    act.wait_ge(l_var, done(1, v - 1))
                    act.wait_ge(l_out, done(1, v0 - 1))
                    passing(act, "act")
                    act.activation(ysq[:], yc[:, bass.ds(c * CH, CH)], ACT.Square).then_inc(l_sq, 1)

                def tail_rs(v):
                    act.wait_ge(l_var, done(1, v))
                    act.wait_ge(l_yn, done(1, v - 1))
                    act.activation(yrs[:], M, ACT.Ln, bias=col("eps")).then_inc(l_ln, 1)
                    act.wait_ge(l_ln, done(1, v))
                    act.activation(yrs[:], yrs[:], ACT.Exp, scale=-0.5).then_inc(l_rs, 1)

                def tail_affine(v, c):
                    act.wait_ge(l_yn, done(1, v))
                    act.wait_ge(l_out, done(1, v - 1))
                    passing(act, "act")
                    act.activation(yg[:], yc[:, bass.ds(c * CH, CH)], ACT.Identity, bias=col("onorm_b"),
                                   scale=col("onorm_g")).then_inc(l_yg, 1)

                def transpose_x(c):
                    passing(act, "act")
                    act.copy(xT[:, bass.ds(c * CH, CH)].rearrange("p (w h) -> p w h", h=H),
                             xN[:].rearrange("p (h w) -> p w h", w=W)[:, bass.ds(c * 8, 8), :]).then_inc(xt_s, 1)

                def body(u, t, par, q, c, nq, n_c, sec):
                    for s in range(1, 9):
                        if s == 8:
                            act.wait_ge(dt_d, done(1, t + 1))
                        decay(t, s, q if s < 8 else nq, par if s < 8 else 1 - par)
                        b_copy(t, s + 2)
                        if sec == 1 and s == 1:
                            transpose_x(c)
                        prep(t + 1, nq, 1 - par, s)
                        if sec == 1 and s == 2:
                            tail_sq(u * NC, c)
                        if sec == 1 and s == 7:
                            tail_rs(u * NC + c)
                        if sec == 2 and s == 8:
                            conv((u + 1) * NC + c, c)
                        if sec == 3 and s == 2:
                            tail_affine(u * NC + c, c)

                with act.Fori(0, NC) as c:
                    conv(c, c)
                for s in (2, 3, 4, 5):
                    prep(0, ORDER[0], 0, s)
                act.wait_ge(dt_d, done(1, 0))
                b_copy(-1, 8)
                decay(-1, 8, ORDER[0], 0)
                b_copy(-1, 9)
                b_copy(-1, 10)
                sections(act, body)
                with act.Fori(0, NC) as c:
                    tail_sq(UNITS * NC, c)
                    tail_rs(c + UNITS * NC)
                with act.Fori(0, NC) as c:
                    tail_affine(c + UNITS * NC, c)

            @block.gpsimd
            def _(pool):
                def delta_b_u(t, s, par):
                    pool.wait_ge(b_cp, done(8, t, s))
                    pool.wait_ge(h_s, done(16, t, 2 * (s - 4) + 1))
                    pool.tensor_tensor(dbu[:, s % 4, :, :], bs[:, s % 4, :, :],
                                       du[:, par:par + 1, :].to_broadcast([P, 2, CH]), ALU.mult).then_inc(dbu_s, 1)

                def prep(t, q, c, par, s):
                    if s == 5:
                        pool.wait_ge(dt_s, done(2, t, 1))
                        pool.tensor_tensor(dw[:], dw[:], da[:], ALU.mult).then_inc(dt_p, 1)
                        pool.wait_ge(dt_relu, done(1, t))
                        pool.wait_ge(dt_p, done(1, t))
                        pool.wait_ge(e_s, done(16, t - 2, 15))
                        pool.tensor_tensor(dl[:, par, :], dq[:], dw[:], ALU.add).then_inc(dt_d, 1)
                        pool.wait_ge(dt_d, done(1, t))
                        passing(pool, "pool")
                        pool.tensor_tensor(du[:, par, :], dl[:, par, :], source(q, c), ALU.mult).then_inc(dt_u, 1)

                def silu(v, c):
                    at = bass.ds(c * CH, CH)
                    pool.wait_ge(cv_s, done(1, v))
                    passing(pool, "pool")
                    pool.tensor_tensor(xN[:, at], xN[:, at], sg[:, at], ALU.mult).then_inc(x_s, 1)

                def tail_norm(v, c):
                    at = bass.ds(c * CH, CH)
                    pool.wait_ge(l_rs, done(1, v))
                    passing(pool, "pool")
                    pool.tensor_tensor(yc[:, at], yc[:, at], yrs[:], ALU.mult).then_inc(l_yn, 1)

                def body(u, t, par, q, c, nq, n_c, sec):
                    for s in range(1, 9):
                        if s == 6:
                            pool.wait_ge(dt_u, done(1, t + 1))
                        delta_b_u(t, s + 2, par if s < 6 else 1 - par)
                        if sec == 1 and s == 5:
                            pool.wait_ge(xt_s, done(1, u * NC + c))
                        if sec == 3 and s == 5:
                            pool.wait_ge(x_s, done(1, (u + 1) * NC + c))
                        prep(t + 1, nq, n_c, 1 - par, s)
                        if sec == 1 and s == 8:
                            tail_norm(u * NC + c, c)
                        if sec == 3 and s == 2:
                            silu((u + 1) * NC + c, c)

                with pool.Fori(0, NC) as c:
                    silu(c, c)
                pool.wait_ge(x_s, done(1, NC - 1))
                prep(0, ORDER[0], 0, 0, 5)
                pool.wait_ge(dt_u, done(1, 0))
                delta_b_u(-1, 8, 0)
                delta_b_u(-1, 9, 0)
                delta_b_u(-1, 10, 0)
                sections(pool, body)
                with pool.Fori(0, NC) as c:
                    tail_norm(c + UNITS * NC, c)

            @block.vector
            def _(dve):
                def scan(t, s, i, q, first):
                    n = 2 * (s % 8) + i
                    dve.wait_ge(e_s, done(16, t, 2 * s + i))
                    if i == 0:
                        dve.wait_ge(dbu_s, done(8, t, s))
                    a, b, o = ex[:, n % 4, :], dbu[:, s % 4, i, :], h[:, n, :]
                    last = CH - 1
                    if q >= 2:
                        a, b, o, last = a[:, ::-1], b[:, ::-1], o[:, ::-1], 0
                    dve.tensor_tensor_scan(o, a, b, 0.0 if first else h[:, n, last:last + 1],
                                           ALU.mult, ALU.add).then_inc(h_s, 1)

                def product(t, s):
                    dve.wait_ge(c_mm, done(8, t, s))
                    dve.wait_ge(h_s, done(16, t, 2 * s + 1))
                    dve.wait_ge(y_mm, done(8, t, s - 2))
                    n = 2 * (s % 8)
                    dve.tensor_tensor(prod[:, s % 2, :, :], h[:, n:n + 2, :], c_ps[:, s % 2, :, 0:CH], ALU.mult)\
                       .then_inc(p_s, 1)

                def prep(t, q, par, s):
                    if s == 3:
                        dve.wait_ge(bc_hi, done(1, t))
                        dve.tensor_tensor(bcr[64:P, :], bcr[64:P, :], bc3[64:P, par, :], ALU.subtract)\
                           .then_inc(bc_r, 1)
                        dve.wait_ge(dt_e, done(1, t))
                        dve.tensor_scalar(dq[:], da[:], SMALL, None, ALU.max).then_inc(dt_c, 1)
                        dve.tensor_scalar(dw[:], da[:], SMALL, None, ALU.min).then_inc(dt_c, 1)
                    if s == 4:
                        dve.wait_ge(bc_mid, done(1, t))
                        dve.tensor_tensor(bc3[96:P, par, :], bcr[96:P, :], bc3[96:P, par, :], ALU.subtract)\
                           .then_inc(bc_lo, 1)
                    if s == 5:
                        dve.wait_ge(dt_x, done(1, t))
                        dve.wait_ge(dt_s, done(2, t, 1))
                        dve.scalar_tensor_tensor(dq[:], dr[:], ln_small[:, 1:2], dq[:], ALU.max, ALU.add)\
                           .then_inc(dt_relu, 1)

                def add_y(t, q, c):
                    dve.wait_ge(y_mm, done(8, t, 7))
                    passing(dve, "dve")
                    p = natural(q, c)
                    if q in (0, 2):
                        to, y = ya[:, bass.ds(p * CH, CH)], Y
                    else:
                        to = ya[:].rearrange("p (h w) -> p w h", w=W)[:, bass.ds(p * 8, 8), :]
                        y = Y.rearrange("p (w h) -> p w h", h=H)
                    if q == 0:
                        ins = dve.scalar_tensor_tensor(to, source(q, c), Ds_sum[:], y, ALU.mult, ALU.add)
                    else:
                        ins = dve.tensor_tensor(to, to, y, ALU.add)
                    ins.then_inc(yev, 1)

                def tail_centre(v, c):
                    at = bass.ds(c * CH, CH)
                    dve.wait_ge(l_mean, done(1, v))
                    dve.tensor_tensor(yc[:, at], ya[:, at], M, ALU.subtract).then_inc(l_yc, 1)

                def add_skip(v, c, slot):
                    dve.wait_ge(l_out, done(1, v))
                    dve.wait_ge(b_store, 16 * v)
                    skip = xs_pad[:].rearrange("p (h w) -> p h w", w=WP)[:, bass.ds(c * 8 + 1, 8), 1:1 + W]
                    dve.scalar_tensor_tensor(bo[:, slot, :].rearrange("p (h w) -> p h w", w=W), skip,
                                             cols[0:DM, COL["skip"]:COL["skip"] + 1],
                                             m_ps[0:DM, 0:CH].rearrange("p (h w) -> p h w", w=W),
                                             ALU.mult, ALU.add).then_inc(l_bo, 1)

                def body(u, t, par, q, c, nq, n_c, sec):
                    last = isinstance(c, int)
                    for s in range(1, 9):
                        sq_, first = (q, False) if s < 8 else (nq, last)
                        scan(t, s, 0, sq_, first)
                        if s < 8:
                            product(t, s - 1)
                        scan(t, s, 1, sq_, first)
                        if s == 7:
                            product(t, 7)
                            if last:
                                edge = CH - 1 if nq < 2 else 0
                                dve.wait_ge(p_s, done(8, t, 7))
                                dve.memset(h[:, 2:N, edge:edge + 1], 0.0).then_inc(h_zero, 1)
                        if s == 8 and last:
                            dve.wait_ge(h_zero, done(K, u, sec))
                        prep(t + 1, nq, 1 - par, s)
                        if sec == 0 and s == 6:
                            tail_centre(u * NC + c, c)
                        if sec == 3 and s == 7:
                            add_skip(u * NC + c, c, (par + 1) % 2)
                    add_y(t, q, c)

                dve.memset(xc_pad[DM:P, LP - 1:LP], 0.0)
                dve.memset(h[:], 0.0)
                dve.memset(ya[:], 0.0).then_inc(zeroed, 1)
                dve.wait_ge(zeroed, 2)
                for s in (3, 4, 5):
                    prep(0, ORDER[0], 0, s)
                scan(-1, 8, 0, ORDER[0], True)
                scan(-1, 8, 1, ORDER[0], True)
                with dve.Fori(0, UNITS) as u:
                    for i, q in enumerate(ORDER):
                        if i == 3:
                            dve.wait_ge(k_load, 16 * u + 16)
                            passing(dve, "dve")
                        with dve.Fori(0, NC // 2) as c2:
                            for a in (0, 1):
                                c = c2 * 2 + a
                                body(u, u * ROUNDS + c + i * NC, (i * NC + a) % 2, q, c, q, c + 1, i)
                        body(u, u * ROUNDS + ((i + 1) * NC - 1), (i * NC + NC - 1) % 2, q, NC - 1,
                             ORDER[(i + 1) % K], 0, i)
                with dve.Fori(0, NC) as c:
                    tail_centre(c + UNITS * NC, c)
                dve.wait_ge(k_load, 16 * UNITS + 16)
                for c in range(NC):
                    add_skip(UNITS * NC + c, c, c % 2)

        with ExitStack() as s:
            xb = sb("xb", [P, 2, NT, CH], scope=s)
            f_xc = sb("f_xc", [P, 2, NT, CH], scope=s)
            f_sq = sb("f_sq", [P, NT, CH], scope=s)
            f_rs = sb("f_rs", [P, 2, CH], scope=s)
            f_xn = sb("f_xn", [P, 2, NT, CH], scope=s)
            f_o = sb("f_o", [P, 2, NT, CH], scope=s)
            fp = s.enter_context(nc.psum_tensor("fp", [P, 8, 512], F32))
            block = s.enter_context(nc.Block())
            mean = lambda p: fp[:, p, 0:CH]
            var = lambda p: fp[:, 2 + p, 0:CH]
            res = lambda p, o: fp[:, 4 + 2 * p + o, 0:CH]
            G = 2 * NC

            def turns(eng, first, second):
                first(0, 0, 0, 0, 0)
                with eng.Fori(0, B // 2) as b2:
                    for j in range(G):
                        n = j + 1
                        nb = (b2 * 2 + n // NC) % B if n == G else b2 * 2 + n // NC
                        first(b2 * G + n, n % 2, b2 * NC + n // 2, nb, n % NC)
                        second(b2 * G + j, j % 2, b2 * NC + j // 2, b2 * 2 + j // NC, j % NC)

            @block.sync
            def _(sp):
                def first(g, p, i, b, c):
                    if not isinstance(g, int):
                        sp.wait_ge(f_cen, done(1, g - 2))
                    sp.dma_start(xb[:, p, :, :], d["bo"][bass.ds(b * C + DM, C), c * CH:(c + 1) * CH]
                                 .rearrange("(t p) l -> p t l", p=P)).then_inc(f_load[p], 16)

                def second(g, p, i, b, c):
                    sp.wait_ge(f_oa, done(1, g))
                    sp.wait_ge(f_ov, done(1, g))
                    sp.dma_start(d["out"][bass.ds(b, 1), :, c * CH:(c + 1) * CH]
                                 .rearrange("a (t p) l -> p (a t) l", p=P), f_o[:, p, :, :]).then_inc(f_store[p], 16)

                turns(sp, first, second)
                for p in (0, 1):
                    sp.wait_ge(f_store[p], 16 * B * NC // 2)
                    sp.wait_ge(f_load[p], 16 * (B * NC // 2 + (1 - p)))

            @block.tensor
            def _(pe):
                def first(g, p, i, b, c):
                    pe.wait_ge(f_load[p], 16 * i + 16)
                    for t in range(NT):
                        mm = pe.matmul(mean(p), ones_c[:], xb[:, p, t, :], start=(t == 0), stop=(t == NT - 1))
                    mm.then_inc(f_mean, 1)

                def second(g, p, i, b, c):
                    pe.wait_ge(f_sqr, done(1, g))
                    for t in range(NT):
                        mm = pe.matmul(var(p), ones_c[:], f_sq[:, t, :], start=(t == 0), stop=(t == NT - 1))
                    mm.then_inc(f_var, 1)
                    pe.wait_ge(f_aff, done(1, g))
                    for o in range(NT):
                        for t in range(NT):
                            mm = pe.matmul(res(p, o), w_proj[:, t, o * P:(o + 1) * P], f_xn[:, p, t, :],
                                           start=(t == 0), stop=(t == NT - 1))
                    mm.then_inc(f_mm, 1)

                turns(pe, first, second)

            @block.vector
            def _(dve):
                def first(g, p, i, b, c):
                    dve.wait_ge(f_mean, done(1, g))
                    for t in range(NT):
                        ins = dve.tensor_tensor(f_xc[:, p, t, :], xb[:, p, t, :], mean(p), ALU.subtract)
                    ins.then_inc(f_cen, 1)

                def second(g, p, i, b, c):
                    dve.wait_ge(f_mm, done(1, g))
                    dve.wait_ge(f_store[p], 16 * i)
                    dve.tensor_scalar(f_o[:, p, 1, :], res(p, 1), col("proj_b", 1), None, ALU.add)\
                       .then_inc(f_ov, 1)

                turns(dve, first, second)

            @block.scalar
            def _(act):
                act.preload_act_table_set(TABLES)
                def first(g, p, i, b, c):
                    pass

                def second(g, p, i, b, c):
                    act.wait_ge(f_cen, done(1, g))
                    act.activation(f_sq[:], f_xc[:, p, :, :], ACT.Square).then_inc(f_sqr, 1)
                    act.wait_ge(f_var, done(1, g))
                    act.activation(f_rs[:, p, :], var(p), ACT.Ln, bias=col("eps")).then_inc(f_ln, 1)
                    act.wait_ge(f_ln, done(1, g))
                    act.activation(f_rs[:, p, :], f_rs[:, p, :], ACT.Exp, scale=-0.5).then_inc(f_rsd, 1)
                    act.wait_ge(f_nrm, done(1, g))
                    for t in range(NT):
                        ins = act.activation(f_xn[:, p, t, :], f_xn[:, p, t, :], ACT.Identity,
                                             bias=col("ln_b", t), scale=col("ln_g", t))
                    ins.then_inc(f_aff, 1)
                    act.wait_ge(f_mm, done(1, g))
                    act.wait_ge(f_store[p], 16 * i)
                    act.activation(f_o[:, p, 0, :], res(p, 0), ACT.Identity, bias=col("proj_b", 0))\
                       .then_inc(f_oa, 1)

                turns(act, first, second)

            @block.gpsimd
            def _(pool):
                with pool.Fori(0, B * NC // 2) as g2:
                    for p in (0, 1):
                        g = g2 * 2 + p
                        pool.wait_ge(f_rsd, done(1, g))
                        pool.wait_ge(f_mm, done(1, g - 2))
                        for t in range(NT):
                            ins = pool.tensor_tensor(f_xn[:, p, t, :], f_xc[:, p, t, :], f_rs[:, p, :], ALU.mult)
                        ins.then_inc(f_nrm, 1)


def kernel(**inputs):
    import numpy as np
    import concourse.bacc as bacc
    from concourse.bass_utils import run_bass_kernel_spmd as run

    a = {n: np.asarray(v) for n, v in inputs.items()}
    f = np.float32

    def tiles(v):
        return np.asarray(v, f).reshape(-1, P).T

    l0, l1 = (lambda n: a["L0_conv_" + n]), (lambda n: a["L1_conv_" + n])
    parts = [tiles(l0("theta_b")), tiles(l0("phi_b")), tiles(l0("g_b")), tiles(l1("conv_b")),
             tiles(l1("onorm_g")), tiles(l1("onorm_b")), np.broadcast_to(l1("skip_scale"), (P, 1)),
             np.full((P, 1), EPS, f), np.full((P, 1), SMALL, f), tiles(l0("out_b")), tiles(l0("bn_gamma")), tiles(l0("bn_beta")),
             tiles(l0("bn_mean")), tiles(l0("bn_var")), tiles(l1("ln_g")), tiles(l1("ln_b")),
             tiles(l1("proj_b")), tiles(l1("dt_b")), tiles(l1("Ds")),
             l1("A_logs").reshape(K, P, N).transpose(1, 0, 2).reshape(P, K * N)]
    sel = np.zeros((P, 2 * N, P), f)
    for j in range(2 * N):
        for q in (0, 64, 96):
            sel[q + j, j, :] = 1.0
    import ml_dtypes
    cw = l1("conv_W").reshape(P, 9).T
    taps = np.zeros((P, 6, P), f)
    for dy in range(3):
        taps[:DM, dy] = cw[3 * dy]
        taps[DM:, dy] = cw[3 * dy + 1]
        taps[:DM, 3 + dy] = cw[3 * dy + 2]
    arrays = {
        "x": a["x"].reshape(B, C, L),
        "cols": np.concatenate(parts, axis=1),
        "ident": np.eye(P, dtype=f),
        "sel": sel.astype(ml_dtypes.bfloat16),
        "xp": l1("x_proj_W").transpose(2, 0, 1),
        "xdt": l1("x_proj_W")[:, :R].transpose(1, 0, 2),
        "dtw": l1("dt_W").transpose(2, 0, 1),
        "inw2": np.concatenate([l1("in_W")] * 2, axis=0),
        "taps": taps,
        "out_W": l1("out_W"),
        "proj_W": l1("proj_W"),
        "thph": np.stack([l0("theta_w").T, l0("phi_w").T, l0("g_w").T], axis=1),
        "w_o": l0("out_w").T,
    }
    arrays = {"in_" + n: np.ascontiguousarray(v) for n, v in arrays.items()}
    nc = bacc.Bacc("TRN2", target_bir_lowering=False, num_devices=1)
    d = {n[3:]: nc.dram_tensor(n, v.shape, mybir.dt.from_np(v.dtype), kind="ExternalInput").ap()
         for n, v in arrays.items()}
    d["xn"] = nc.dram_tensor("scratch_xn", (B * C, LP), F32, kind="Internal").ap()
    d["bo"] = nc.dram_tensor("scratch_bo", ((UNITS + 1) * DM, L), F32, kind="Internal").ap()
    d["out"] = nc.dram_tensor("out", (B, C, L), F32, kind="ExternalOutput").ap()
    build(nc, d)
    r = run(nc, [arrays], core_ids=[0])
    return r.results[0]["out"].reshape(B, C, H, W)
```
